# Optimizing a Trainium2 kernel written in Bass

```python
import numpy as np
import jax
import jax.numpy as jnp

def _softmax(x, axis=-1):
    return jax.nn.softmax(x, axis=axis)

def _gelu(x):
    return jax.nn.gelu(x, approximate=True)

def _silu(x):
    return jax.nn.silu(x)

def _sigmoid(x):
    return jax.nn.sigmoid(x)

def _layernorm(x, axis=-1, eps=1e-05):
    m = jnp.mean(x, axis=axis, keepdims=True)
    v = jnp.var(x, axis=axis, keepdims=True)
    return (x - m) / jnp.sqrt(v + eps)

def _scatter_add(tgt, idx, src, axis=0):
    return tgt.at[idx].add(src)

def _segment_sum(src, seg, n):
    return jax.ops.segment_sum(src, seg, n)
kernel_name = 'mk_dlrm_tower_d1_rec_r8_270b8a'

def setup_inputs(seed: int=0):
    np.random.seed(seed)
    _w = jnp.asarray

    def _rec_inputs():
        import jax
        import jax.numpy as jnp
        _tk = jax.random.key(seed)
        dense_ctx = jax.random.normal(jax.random.fold_in(_tk, 190), (2048, 16), jnp.float32)
        ids = jnp.stack([jax.random.randint(jax.random.fold_in(_tk, 200 + f), (2048,), 0, v, jnp.int32) for f, v in enumerate([12500, 1250, 1250, 125000, 1250, 1000, 12500, 1250, 1250, 12500, 1250, 1000, 12500, 12500, 1250, 1000, 12500, 1000, 1000, 12500, 1250, 12500, 1250, 1250, 1000, 1000, 1000])], axis=1)
        tbl_0 = 0.05 * jax.random.normal(jax.random.fold_in(_tk, 500 + 0), (12500, 128), jnp.float32)
        tbl_1 = 0.05 * jax.random.normal(jax.random.fold_in(_tk, 500 + 1), (1250, 128), jnp.float32)
        tbl_2 = 0.05 * jax.random.normal(jax.random.fold_in(_tk, 500 + 2), (1250, 128), jnp.float32)
        tbl_3 = 0.05 * jax.random.normal(jax.random.fold_in(_tk, 500 + 3), (125000, 128), jnp.float32)
        tbl_4 = 0.05 * jax.random.normal(jax.random.fold_in(_tk, 500 + 4), (1250, 128), jnp.float32)
        tbl_5 = 0.05 * jax.random.normal(jax.random.fold_in(_tk, 500 + 5), (1000, 128), jnp.float32)
        tbl_6 = 0.05 * jax.random.normal(jax.random.fold_in(_tk, 500 + 6), (12500, 128), jnp.float32)
        tbl_7 = 0.05 * jax.random.normal(jax.random.fold_in(_tk, 500 + 7), (1250, 128), jnp.float32)
        tbl_8 = 0.05 * jax.random.normal(jax.random.fold_in(_tk, 500 + 8), (1250, 128), jnp.float32)
        tbl_9 = 0.05 * jax.random.normal(jax.random.fold_in(_tk, 500 + 9), (12500, 128), jnp.float32)
        tbl_10 = 0.05 * jax.random.normal(jax.random.fold_in(_tk, 500 + 10), (1250, 128), jnp.float32)
        tbl_11 = 0.05 * jax.random.normal(jax.random.fold_in(_tk, 500 + 11), (1000, 128), jnp.float32)
        tbl_12 = 0.05 * jax.random.normal(jax.random.fold_in(_tk, 500 + 12), (12500, 128), jnp.float32)
        tbl_13 = 0.05 * jax.random.normal(jax.random.fold_in(_tk, 500 + 13), (12500, 128), jnp.float32)
        tbl_14 = 0.05 * jax.random.normal(jax.random.fold_in(_tk, 500 + 14), (1250, 128), jnp.float32)
        tbl_15 = 0.05 * jax.random.normal(jax.random.fold_in(_tk, 500 + 15), (1000, 128), jnp.float32)
        tbl_16 = 0.05 * jax.random.normal(jax.random.fold_in(_tk, 500 + 16), (12500, 128), jnp.float32)
        tbl_17 = 0.05 * jax.random.normal(jax.random.fold_in(_tk, 500 + 17), (1000, 128), jnp.float32)
        tbl_18 = 0.05 * jax.random.normal(jax.random.fold_in(_tk, 500 + 18), (1000, 128), jnp.float32)
        tbl_19 = 0.05 * jax.random.normal(jax.random.fold_in(_tk, 500 + 19), (12500, 128), jnp.float32)
        tbl_20 = 0.05 * jax.random.normal(jax.random.fold_in(_tk, 500 + 20), (1250, 128), jnp.float32)
        tbl_21 = 0.05 * jax.random.normal(jax.random.fold_in(_tk, 500 + 21), (12500, 128), jnp.float32)
        tbl_22 = 0.05 * jax.random.normal(jax.random.fold_in(_tk, 500 + 22), (1250, 128), jnp.float32)
        tbl_23 = 0.05 * jax.random.normal(jax.random.fold_in(_tk, 500 + 23), (1250, 128), jnp.float32)
        tbl_24 = 0.05 * jax.random.normal(jax.random.fold_in(_tk, 500 + 24), (1000, 128), jnp.float32)
        tbl_25 = 0.05 * jax.random.normal(jax.random.fold_in(_tk, 500 + 25), (1000, 128), jnp.float32)
        tbl_26 = 0.05 * jax.random.normal(jax.random.fold_in(_tk, 500 + 26), (1000, 128), jnp.float32)
        _rk = jax.random.fold_in(_tk, 7)
        W_top1 = 0.0521996 * jax.random.normal(jax.random.fold_in(_tk, 801), (367, 512), jnp.float32)
        W_top2 = 0.0441942 * jax.random.normal(jax.random.fold_in(_tk, 802), (512, 256), jnp.float32)
        W_top3 = 0.0625 * jax.random.normal(jax.random.fold_in(_tk, 803), (256, 1), jnp.float32)
        b_top1 = jnp.zeros((512,), jnp.float32)
        b_top2 = jnp.zeros((256,), jnp.float32)
        return (dense_ctx, ids, tbl_0, tbl_1, tbl_2, tbl_3, tbl_4, tbl_5, tbl_6, tbl_7, tbl_8, tbl_9, tbl_10, tbl_11, tbl_12, tbl_13, tbl_14, tbl_15, tbl_16, tbl_17, tbl_18, tbl_19, tbl_20, tbl_21, tbl_22, tbl_23, tbl_24, tbl_25, tbl_26, W_top1, b_top1, W_top2, b_top2, W_top3)
    dense_ctx, ids, tbl_0, tbl_1, tbl_2, tbl_3, tbl_4, tbl_5, tbl_6, tbl_7, tbl_8, tbl_9, tbl_10, tbl_11, tbl_12, tbl_13, tbl_14, tbl_15, tbl_16, tbl_17, tbl_18, tbl_19, tbl_20, tbl_21, tbl_22, tbl_23, tbl_24, tbl_25, tbl_26, W_top1, b_top1, W_top2, b_top2, W_top3 = _rec_inputs()

    def _L0_rec_setup():
        import jax, jax.numpy as jnp
        import numpy as np

        def _tri_indices(num_feas):
            return np.array([i * num_feas + j for j in range(1, num_feas) for i in range(j)], dtype=np.int32)
        key = jax.random.key(seed)
        batch, num_feas, embed_dim = (2048, 27, 128)
        inputs = jax.random.normal(key, (batch, num_feas, embed_dim), dtype=jnp.float32)
        return {'inputs': inputs, 'num_feas': num_feas}
    _L0_rec_all = _L0_rec_setup()
    _L0_rec_in = {k: v for k, v in _L0_rec_all.items() if k in ()}
    del _L0_rec_all
    return {'dense_ctx': dense_ctx, 'ids': ids, 'tbl_0': tbl_0, 'tbl_1': tbl_1, 'tbl_2': tbl_2, 'tbl_3': tbl_3, 'tbl_4': tbl_4, 'tbl_5': tbl_5, 'tbl_6': tbl_6, 'tbl_7': tbl_7, 'tbl_8': tbl_8, 'tbl_9': tbl_9, 'tbl_10': tbl_10, 'tbl_11': tbl_11, 'tbl_12': tbl_12, 'tbl_13': tbl_13, 'tbl_14': tbl_14, 'tbl_15': tbl_15, 'tbl_16': tbl_16, 'tbl_17': tbl_17, 'tbl_18': tbl_18, 'tbl_19': tbl_19, 'tbl_20': tbl_20, 'tbl_21': tbl_21, 'tbl_22': tbl_22, 'tbl_23': tbl_23, 'tbl_24': tbl_24, 'tbl_25': tbl_25, 'tbl_26': tbl_26, 'W_top1': W_top1, 'b_top1': b_top1, 'W_top2': W_top2, 'b_top2': b_top2, 'W_top3': W_top3}

def reference(dense_ctx, ids, tbl_0, tbl_1, tbl_2, tbl_3, tbl_4, tbl_5, tbl_6, tbl_7, tbl_8, tbl_9, tbl_10, tbl_11, tbl_12, tbl_13, tbl_14, tbl_15, tbl_16, tbl_17, tbl_18, tbl_19, tbl_20, tbl_21, tbl_22, tbl_23, tbl_24, tbl_25, tbl_26, W_top1, b_top1, W_top2, b_top2, W_top3):
    import jax
    import jax.numpy as jnp

    def _L0_rec_ref(inputs, num_feas):
        import jax, jax.numpy as jnp
        import numpy as np

        def _tri_indices(num_feas):
            return np.array([i * num_feas + j for j in range(1, num_feas) for i in range(j)], dtype=np.int32)
        dot = jnp.einsum('bnd,bmd->bnm', inputs, inputs)
        idx = jnp.asarray(_tri_indices(num_feas))
        flat = dot.reshape(inputs.shape[0], num_feas * num_feas)
        return flat[:, idx]
    e = jnp.stack([tbl_0[ids[:, 0]], tbl_1[ids[:, 1]], tbl_2[ids[:, 2]], tbl_3[ids[:, 3]], tbl_4[ids[:, 4]], tbl_5[ids[:, 5]], tbl_6[ids[:, 6]], tbl_7[ids[:, 7]], tbl_8[ids[:, 8]], tbl_9[ids[:, 9]], tbl_10[ids[:, 10]], tbl_11[ids[:, 11]], tbl_12[ids[:, 12]], tbl_13[ids[:, 13]], tbl_14[ids[:, 14]], tbl_15[ids[:, 15]], tbl_16[ids[:, 16]], tbl_17[ids[:, 17]], tbl_18[ids[:, 18]], tbl_19[ids[:, 19]], tbl_20[ids[:, 20]], tbl_21[ids[:, 21]], tbl_22[ids[:, 22]], tbl_23[ids[:, 23]], tbl_24[ids[:, 24]], tbl_25[ids[:, 25]], tbl_26[ids[:, 26]]], axis=1)
    z = _L0_rec_ref(e, 27)
    z = z.reshape(z.shape[0], -1)
    h = jnp.concatenate([z, dense_ctx], axis=1)
    h = jnp.maximum(h @ W_top1 + b_top1, 0.0)
    h = jnp.maximum(h @ W_top2 + b_top2, 0.0)
    y = h @ W_top3
    return y

_drawn_inputs = setup_inputs


def setup_inputs(seed=0):
    import zlib

    import numpy as np

    out = dict(_drawn_inputs(seed))
    spreads = {'b_top1': (0.0, 0.1), 'b_top2': (0.0, 0.1)}
    factors = {}
    for name, (base, spread) in spreads.items():
        noise = np.random.default_rng([zlib.crc32(name.encode()), seed]).standard_normal(out[name].shape)
        drawn = base * np.exp(spread * noise) if base else spread * noise
        out[name] = jnp.asarray(drawn.astype(out[name].dtype))
    for name, factor in factors.items():
        out[name] = (out[name] * factor).astype(out[name].dtype)
    return out
```

```python
import numpy as np

SAMPLES, DIM, FEATURES, DENSE = 2048, 128, 27, 16
TILE, TILES_PER_SLAB = 128, 4
SLAB = TILE * TILES_PER_SLAB
SLABS = SAMPLES // SLAB
GROUPS, GROUP = 4, 32
HALF = GROUP // 2

PICKED = [5, 11, 15, 17, 18, 24, 25, 26]
GATHERED = [f for f in range(FEATURES) if f not in PICKED]
NP, NG = len(PICKED), len(GATHERED)
ORDER = GATHERED + PICKED
ROWS, CHUNKS = 1000, 8
CHUNK = ROWS // CHUNKS

SHIFTS = (FEATURES - 1) // 2
WRAPPED = FEATURES + SHIFTS
PARTS = 3
ANCHORS = FEATURES // PARTS
PAIRS = ANCHORS * SHIFTS
DENSE_IN = [8, 8, 0]
PART_ROWS = [PAIRS + d for d in DENSE_IN]
H1, H2 = 512, 256
H1C, H2C = H1 // 128, H2 // 128

PER_BANK = 4
BANKFULS = [GATHERED[a:a + PER_BANK] for a in range(0, NG, PER_BANK)]
NB = len(BANKFULS)
RING = 4
RAW = 3
MLP = H1C + H2C + 1


def first_layer_rows():
    rows = []
    dense = FEATURES * (FEATURES - 1) // 2
    for part in range(PARTS):
        for i in range(part * ANCHORS, (part + 1) * ANCHORS):
            for k in range(1, SHIFTS + 1):
                a, b = sorted((ORDER[i], ORDER[(i + k) % FEATURES]))
                rows.append(b * (b - 1) // 2 + a)
        rows += range(dense, dense + DENSE_IN[part])
        dense += DENSE_IN[part]
    return rows


def constants():
    ident = np.eye(128, dtype=np.float32)
    row_of = (CHUNKS * np.arange(CHUNK)[:, None] + np.arange(CHUNKS)[None, :]).astype(np.float32)
    spread = np.repeat(np.eye(NP, dtype=np.float32)[:, :, None], CHUNK, axis=2).reshape(NP, NP * CHUNK)
    return ident, row_of, np.ascontiguousarray(spread)


def build(nc, ids, picked_ids, tables, denseT, w1, b1, w2, b2, w3, ident_in, row_of_in, spread_in, out):
    from contextlib import ExitStack

    import concourse.bass as bass
    from concourse import mybir
    from concourse.alu_op_type import AluOpType as ALU

    F32, F32R, I32, U32 = mybir.dt.float32, mybir.dt.float32r, mybir.dt.int32, mybir.dt.uint32
    ACT = mybir.ActivationFunctionType

    grams = nc.dram_tensor("grams", [FEATURES, WRAPPED, SLAB], F32, kind="Internal").ap()
    Q = SLAB // GROUPS

    ctx = ExitStack()
    with ctx:
        def sb(name, shape, dt=F32):
            return ctx.enter_context(nc.sbuf_tensor(name, shape, dt))

        def pb(name):
            return ctx.enter_context(nc.psum_tensor(name, [128, 512], F32))

        def sem(name):
            return ctx.enter_context(nc.semaphore(name))

        ident = sb("ident", [128, 128])
        row_of = sb("row_of", [CHUNK, CHUNKS])
        spread_raw = sb("spread_raw", [NP, NP * CHUNK])
        spread = sb("spread", [NP, NP * CHUNK], F32R)
        pids_raw = sb("pids_raw", [NP, SAMPLES], I32)
        pids = sb("pids", [NP, SAMPLES], F32R)
        index = sb("index", [128, TILES_PER_SLAB, FEATURES], I32)
        rows = sb("rows", [128, 2, NG, DIM])
        hi = sb("hi", [CHUNK, NP, CHUNKS * DIM], F32R)
        lo = sb("lo", [CHUNK, NP, CHUNKS * DIM], F32R)
        onehot = sb("onehot", [CHUNK, RING, SLAB], F32R)
        pickedT = sb("pickedT", [128, 2, NP, SLAB])
        eT = sb("eT", [128, TILE, FEATURES])
        z = sb("z", [128, FEATURES, Q])
        raw = z[:, :, :].rearrange("p j q -> p (j q)")
        zT = sb("zT", [max(PART_ROWS), PARTS, SLAB])
        w1s = sb("w1s", [max(PART_ROWS), PARTS, H1])
        w2s = sb("w2s", [128, H1C, H2])
        w3s = sb("w3s", [128, H2C])
        b1s = sb("b1s", [128, H1C])
        b2s = sb("b2s", [128, H2C])
        h1 = sb("h1", [128, H1C, SLAB])
        h2 = sb("h2", [128, H2C, SLAB])
        ys = sb("ys", [1, SLAB])

        turned = [pb(f"turned{k}") for k in range(2)]
        idb = [pb(f"idb{k}") for k in range(2)]
        pick = pb("pick")
        dots = [pb(f"dots{k}") for k in range(2)]
        layer = pb("layer")

        index_loaded = [sem(f"index_loaded{t}") for t in range(TILES_PER_SLAB)]
        gathered = [sem(f"gathered{k}") for k in range(2)]
        ident_loaded = sem("ident_loaded")
        small_loaded = sem("small_loaded")
        weights_loaded = sem("weights_loaded")
        raw_loaded = [sem(f"raw_loaded{k}") for k in range(RAW)]
        hi_split, lo_split = sem("hi_split"), sem("lo_split")
        ids_ready, dots_cleared = sem("ids_ready"), sem("dots_cleared")
        turned_filled, turned_copied = sem("turned_filled"), sem("turned_copied")
        idb_filled = sem("idb_filled")
        onehot_ready, onehot_used = sem("onehot_ready"), sem("onehot_used")
        pick_copied, picked_placed = sem("pick_copied"), sem("picked_placed")
        dots_filled, dots_copied = sem("dots_filled"), sem("dots_copied")
        grams_stored, zT_loaded = sem("grams_stored"), sem("zT_loaded")
        layer_filled, layer_copied = sem("layer_filled"), sem("layer_copied")
        y_stored = sem("y_stored")
        waited = sem("waited")

        GRAM_STORES, ZT_LOADS = 2 * GROUPS, PARTS + 2

        block = ctx.enter_context(nc.Block())

        @block.gpsimd
        def _(pool):
            def slab(s, first):
                for t in range(TILES_PER_SLAB):
                    n = s * TILES_PER_SLAB + t
                    pool.wait_ge(index_loaded[t], 16 * (s + 1))
                    if not (first and t < 2):
                        pool.wait_ge(turned_filled, NB * (n - 1))
                    pool.sem_inc(waited, 1)
                    for a, f in enumerate(GATHERED):
                        pool.indirect_dma_start(
                            rows[:, t % 2, a, :], None, tables[f],
                            bass.IndirectOffsetOnAxis(ap=index[:, t, f:f + 1].bitcast(U32), axis=0),
                        ).then_inc(gathered[t % 2], 16)

            slab(0, True)
            with pool.Fori(1, SLABS) as s:
                slab(s, False)

        @block.sync
        def _(sp):
            by_tile = ids.rearrange("(n p) f -> p n f", p=TILE)
            for t in range(TILES_PER_SLAB):
                sp.dma_start(index[:, t, :], by_tile[:, t, :]).then_inc(index_loaded[t], 16)
            for k, f in enumerate(PICKED):
                if k >= RAW:
                    sp.wait_ge(hi_split, k - RAW + 1)
                    sp.wait_ge(lo_split, k - RAW + 1)
                sp.dma_start(raw[0:CHUNK, (k % RAW) * CHUNKS * DIM:(k % RAW + 1) * CHUNKS * DIM],
                             tables[f].rearrange("(p c) d -> p (c d)", c=CHUNKS)).then_inc(raw_loaded[k % RAW], 16)

            def next_indices(s):
                for t in range(TILES_PER_SLAB):
                    sp.wait_ge(gathered[t % 2], 16 * NG * (2 * s + t // 2 + 1))
                    sp.sem_inc(waited, 1)
                    sp.dma_start(index[:, t, :], by_tile[:, bass.ds((s + 1) * TILES_PER_SLAB + t, 1), :]
                                 .rearrange("p n f -> p (n f)")).then_inc(index_loaded[t], 16)

            def pairs_to_partitions(s, first):
                sp.wait_ge(dots_copied, 2 * TILES_PER_SLAB * (s + 1))
                sp.sem_inc(waited, 1)
                if not first:
                    sp.wait_ge(zT_loaded, 16 * ZT_LOADS * s)
                for g in range(GROUPS):
                    for at, width in ((0, FEATURES), (FEATURES, SHIFTS)):
                        sp.dma_start(grams[:, at:at + width, g * Q:(g + 1) * Q],
                                     z[g * 32:g * 32 + FEATURES, 0:width, :]).then_inc(grams_stored, 16)
                if not first:
                    sp.wait_ge(layer_filled, MLP * (s - 1) + H1C)
                    sp.sem_inc(waited, 1)
                at = 0
                for part, d in enumerate(DENSE_IN):
                    if d:
                        sp.dma_start(zT[PAIRS:PAIRS + d, part, :], denseT[at:at + d, bass.ds(s * SLAB, SLAB)])\
                          .then_inc(zT_loaded, 16)
                        at += d
                sp.wait_ge(grams_stored, 16 * GRAM_STORES * (s + 1))
                for part in range(PARTS):
                    i = part * ANCHORS
                    src = bass.AP(grams.tensor, (i * WRAPPED + i + 1) * SLAB,
                                  [[(WRAPPED + 1) * SLAB, ANCHORS], [SLAB, SHIFTS], [1, SLAB]])
                    sp.dma_start(zT[0:PAIRS, part, :], src).then_inc(zT_loaded, 16)

            def store_y(s):
                sp.wait_ge(layer_copied, MLP * (s + 1))
                sp.sem_inc(waited, 1)
                dst = out[bass.ds(s * SLAB, SLAB), :].rearrange("(t g q) o -> o g t q", t=TILES_PER_SLAB, g=GROUPS)
                sp.dma_start(dst, ys[:, :].rearrange("o (g t q) -> o g t q", g=GROUPS, t=TILES_PER_SLAB))\
                  .then_inc(y_stored, 16)

            next_indices(0)
            pairs_to_partitions(0, True)
            with sp.Fori(1, SLABS - 1) as s:
                next_indices(s)
                store_y(s - 1)
                pairs_to_partitions(s, False)
            store_y(SLABS - 2)
            pairs_to_partitions(SLABS - 1, False)
            store_y(SLABS - 1)
            sp.wait_ge(y_stored, 16 * SLABS)

        @block.scalar
        def _(act):
            act.dma_start(ident[:, :], ident_in).then_inc(ident_loaded, 16)
            for dst, src in ((row_of, row_of_in), (spread_raw, spread_in), (pids_raw, picked_ids)):
                act.dma_start(dst[:, :], src).then_inc(small_loaded, 16)
            at = 0
            for part, r in enumerate(PART_ROWS):
                act.dma_start(w1s[0:r, part, :], w1[at:at + r, :]).then_inc(weights_loaded, 16)
                at += r
            act.dma_start(w2s[:, :, :], w2.rearrange("(c p) n -> p c n", p=128)).then_inc(weights_loaded, 16)
            act.dma_start(w3s[:, :], w3).then_inc(weights_loaded, 16)
            act.dma_start(b1s[:, :], b1).then_inc(weights_loaded, 16)
            act.dma_start(b2s[:, :], b2).then_inc(weights_loaded, 16)

            def copy_turned(s, t, first):
                n = s * TILES_PER_SLAB + t
                if not first:
                    act.wait_ge(dots_filled, 2 * n)
                for j, fs in enumerate(BANKFULS):
                    act.wait_ge(turned_filled, NB * n + j + 1)
                    a = j * PER_BANK
                    nc.scalar.copy(eT[:, :, a:a + len(fs)].rearrange("p b f -> p f b"),
                                   turned[(NB * t + j) % 2][:, 0:len(fs) * TILE]
                                   .rearrange("p (f b) -> p f b", f=len(fs))).then_inc(turned_copied, 1)

            def place_picked(s, t):
                act.wait_ge(pick_copied, NP * (s + 1))
                nc.scalar.copy(eT[:, :, NG:FEATURES].rearrange("p b f -> p f b"),
                               pickedT[:, bass.ds(s % 2, 1), :, t * TILE:(t + 1) * TILE]
                               .rearrange("p o f b -> p (o f) b")).then_inc(picked_placed, 1)

            def copy_pick(s, k):
                act.wait_ge(onehot_used, CHUNKS * (NP * s + k + 1))
                nc.scalar.copy(pickedT[:, bass.ds(s % 2, 1), k, :].rearrange("p o b -> p (o b)"), pick[:, :])\
                  .then_inc(pick_copied, 1)

            def copy_layer(s, m):
                act.wait_ge(layer_filled, MLP * s + m + 1)
                if m < H1C:
                    op = nc.scalar.activation(h1[:, m, :], layer[:, :], ACT.Relu, bias=b1s[:, m:m + 1])
                elif m < H1C + H2C:
                    op = nc.scalar.activation(h2[:, m - H1C, :], layer[:, :], ACT.Relu, bias=b2s[:, m - H1C:m - H1C + 1])
                else:
                    if not isinstance(s, int) or s > 0:
                        act.wait_ge(y_stored, 16 * s)
                    op = nc.scalar.copy(ys[:, :], layer[0:1, :])
                op.then_inc(layer_copied, 1)

            def copy_dots(s, t, first):
                n = s * TILES_PER_SLAB + t
                if t == 0 and not first:
                    act.wait_ge(grams_stored, 16 * GRAM_STORES * s)
                for h in range(2):
                    act.wait_ge(dots_filled, 2 * n + h + 1)
                    q = t * GROUP + h * HALF
                    nc.scalar.copy(z[:, :, q:q + HALF].rearrange("p j q -> p q j"),
                                   dots[h][:, 0:HALF * FEATURES].rearrange("p (q j) -> p q j", q=HALF))\
                      .then_inc(dots_copied, 1)

            def slab(s, first, last):
                for t in range(TILES_PER_SLAB):
                    if not (first and t == 0):
                        copy_turned(s, t, False)
                    place_picked(s, t)
                    for part in range(2):
                        if not last:
                            copy_pick(s + 1, 2 * t + part)
                        m = 2 * t + part - 1
                        if not first and m >= 0:
                            copy_layer(s - 1, m)
                    copy_dots(s, t, first)

            for k in range(NP):
                act.wait_ge(raw_loaded[k % RAW], 16 * (k // RAW + 1))
                nc.scalar.copy(hi[:, k, :], raw[0:CHUNK, (k % RAW) * CHUNKS * DIM:(k % RAW + 1) * CHUNKS * DIM])\
                  .then_inc(hi_split, 1)
                if k >= 2:
                    copy_pick(0, k - 2)
                if k == 6:
                    copy_turned(0, 0, True)
            copy_pick(0, NP - 2)
            copy_pick(0, NP - 1)
            act.wait_ge(weights_loaded, 16 * (PARTS + 4))
            slab(0, True, False)
            with act.Fori(1, SLABS - 1) as s:
                slab(s, False, False)
            slab(SLABS - 1, False, True)
            for m in range(MLP):
                copy_layer(SLABS - 1, m)

        @block.vector
        def _(dve):
            for d in dots:
                nc.vector.memset(d[:, :], 0.0).then_inc(dots_cleared, 1)
            dve.wait_ge(small_loaded, 48)
            nc.vector.tensor_copy(spread[:, :], spread_raw[:, :]).then_inc(ids_ready, 1)
            nc.vector.tensor_copy(pids[:, :], pids_raw[:, :]).then_inc(ids_ready, 1)

            def one_hots(s, k, first):
                m = NP * s + k
                dve.wait_ge(idb_filled, m + 1)
                for c in range(CHUNKS):
                    if not (first and CHUNKS * k + c < RING):
                        dve.wait_ge(onehot_used, CHUNKS * m + c + 1 - RING)
                    nc.vector.tensor_scalar(onehot[:, c % RING, :], idb[k % 2][0:CHUNK, :], row_of[:, c:c + 1], None,
                                            ALU.is_equal).then_inc(onehot_ready, 1)

            for k in range(NP):
                dve.wait_ge(hi_split, k + 1)
                nc.vector.tensor_tensor(lo[:, k, :], raw[0:CHUNK, (k % RAW) * CHUNKS * DIM:(k % RAW + 1) * CHUNKS * DIM],
                                        hi[:, k, :].bitcast(F32), ALU.subtract).then_inc(lo_split, 1)
                one_hots(0, k, True)
            with dve.Fori(1, SLABS) as s:
                for k in range(NP):
                    one_hots(s, k, False)

        @block.tensor
        def _(pe):
            def turn(s, t, first):
                n = s * TILES_PER_SLAB + t
                pe.wait_ge(gathered[t % 2], 16 * NG * (2 * s + t // 2 + 1))
                for j, fs in enumerate(BANKFULS):
                    if not (first and j < 2):
                        pe.wait_ge(turned_copied, NB * n + j - 1)
                    for c in range(len(fs)):
                        op = nc.tensor.transpose(turned[(NB * t + j) % 2][:, c * TILE:(c + 1) * TILE],
                                                 rows[:, t % 2, j * PER_BANK + c, :], ident[:, :])
                    op.then_inc(turned_filled, 1)

            def spread_ids(s, k, first):
                m = NP * s + k
                if not (first and k < 2):
                    pe.wait_ge(onehot_ready, CHUNKS * (m - 1))
                    pe.sem_inc(waited, 1)
                nc.tensor.matmul(idb[k % 2][0:CHUNK, :], spread[:, k * CHUNK:(k + 1) * CHUNK],
                                 pids[:, bass.ds(s * SLAB, SLAB)], start=True, stop=True).then_inc(idb_filled, 1)

            def pick_feature(s, k, first):
                m = NP * s + k
                if k + 1 < NP:
                    spread_ids(s, k + 1, first)
                if not (first and k == 0):
                    pe.wait_ge(pick_copied, m)
                if first:
                    pe.wait_ge(lo_split, k + 1)
                for c in range(CHUNKS):
                    pe.wait_ge(onehot_ready, CHUNKS * m + c + 1)
                    part = slice(c * DIM, (c + 1) * DIM)
                    nc.tensor.matmul(pick[:, :], hi[:, k, part], onehot[:, c % RING, :], start=c == 0, stop=False)
                    nc.tensor.matmul(pick[:, :], lo[:, k, part], onehot[:, c % RING, :], start=False,
                                     stop=c == CHUNKS - 1).then_inc(onehot_used, 1)

            def dot_products(s, t, first):
                n = s * TILES_PER_SLAB + t
                pe.wait_ge(turned_copied, NB * (n + 1))
                pe.wait_ge(picked_placed, n + 1)
                for h in range(2):
                    if first and t == 0:
                        pe.wait_ge(dots_cleared, h + 1)
                    else:
                        pe.wait_ge(dots_copied, 2 * n + h - 1)
                    for q in range(HALF):
                        for g in range(GROUPS):
                            b = g * GROUP + h * HALF + q
                            op = nc.tensor.matmul(dots[h][g * 32:g * 32 + FEATURES, q * FEATURES:(q + 1) * FEATURES],
                                                  eT[:, b, :], eT[:, b, :], start=True, stop=True,
                                                  tile_position=(0, 32 * g))
                    op.then_inc(dots_filled, 1)

            def dense_layer(s, m):
                if m == 0:
                    pe.wait_ge(zT_loaded, 16 * ZT_LOADS * (s + 1))
                if not (isinstance(s, int) and s == 0 and m == 0):
                    pe.wait_ge(layer_copied, MLP * s + m)
                if m < H1C:
                    terms = [(w1s[0:r, p, m * 128:(m + 1) * 128], zT[0:r, p, :]) for p, r in enumerate(PART_ROWS)]
                    to = layer[:, :]
                elif m < H1C + H2C:
                    a = (m - H1C) * 128
                    terms = [(w2s[:, c, a:a + 128], h1[:, c, :]) for c in range(H1C)]
                    to = layer[:, :]
                else:
                    terms = [(w3s[:, c:c + 1], h2[:, c, :]) for c in range(H2C)]
                    to = layer[0:1, :]
                for i, (w, x) in enumerate(terms):
                    op = nc.tensor.matmul(to, w, x, start=i == 0, stop=i == len(terms) - 1)
                op.then_inc(layer_filled, 1)

            def slab(s, first, last):
                if not last:
                    spread_ids(s + 1, 0, False)
                for t in range(TILES_PER_SLAB):
                    if not (first and t == 0):
                        turn(s, t, False)
                    for part in range(2):
                        if not last:
                            pick_feature(s + 1, 2 * t + part, False)
                        m = 2 * t + part - 1
                        if not first and m >= 0:
                            dense_layer(s - 1, m)
                    dot_products(s, t, first)

            pe.wait_ge(ids_ready, 2)
            spread_ids(0, 0, True)
            for k in range(NP):
                pick_feature(0, k, True)
                if k == 5:
                    pe.wait_ge(ident_loaded, 16)
                    turn(0, 0, True)
            pe.wait_ge(weights_loaded, 16 * (PARTS + 4))
            slab(0, True, False)
            with pe.Fori(1, SLABS - 1) as s:
                slab(s, False, False)
            slab(SLABS - 1, False, True)
            for m in range(MLP):
                dense_layer(SLABS - 1, m)


def kernel(**inputs):
    import concourse.bacc as bacc
    from concourse import mybir
    from concourse.bass_utils import run_bass_kernel_spmd

    nc = bacc.Bacc("TRN2", target_bir_lowering=False, num_devices=1)
    ids = np.ascontiguousarray(inputs["ids"])
    w1 = np.asarray(inputs["W_top1"])
    ident, row_of, spread = constants()
    arrays = {
        "ids": ids,
        "picked_ids": np.ascontiguousarray(ids.T[PICKED]),
        "denseT": np.ascontiguousarray(np.asarray(inputs["dense_ctx"])
                                       .reshape(SLABS, TILES_PER_SLAB, GROUPS, GROUP, DENSE)
                                       .transpose(4, 0, 2, 1, 3).reshape(DENSE, SAMPLES)),
        "w1": np.ascontiguousarray(w1[first_layer_rows()]),
        "b1": np.ascontiguousarray(np.asarray(inputs["b_top1"]).reshape(H1C, 128).T),
        "w2": np.ascontiguousarray(inputs["W_top2"]),
        "b2": np.ascontiguousarray(np.asarray(inputs["b_top2"]).reshape(H2C, 128).T),
        "w3": np.ascontiguousarray(np.asarray(inputs["W_top3"]).reshape(H2C, 128).T),
        "ident_in": ident, "row_of_in": row_of, "spread_in": spread,
    }
    arrays |= {f"tbl_{f}": np.ascontiguousarray(inputs[f"tbl_{f}"]) for f in range(FEATURES)}
    aps = {n: nc.dram_tensor(f"in_{n}", a.shape, mybir.dt.from_np(a.dtype), kind="ExternalInput").ap()
           for n, a in arrays.items()}
    tables = [aps.pop(f"tbl_{f}") for f in range(FEATURES)]
    out = nc.dram_tensor("out_y", [SAMPLES, 1], mybir.dt.float32, kind="ExternalOutput").ap()
    build(nc, tables=tables, out=out, **aps)
    result = run_bass_kernel_spmd(nc, [{f"in_{n}": a for n, a in arrays.items()}], core_ids=[0])
    return result.results[0]["out_y"]
```

```python
import numpy as np

SAMPLES, DIM, FEATURES, DENSE = 2048, 128, 27, 16
TILE, TILES_PER_SLAB = 128, 4
SLAB = TILE * TILES_PER_SLAB
SLABS = SAMPLES // SLAB
GROUPS, GROUP = 4, 32
HALF = GROUP // 2

PICKED_ROWS = {5: 1000, 11: 1000, 15: 1000, 17: 1000, 18: 1000, 24: 1000, 25: 1000, 26: 1000}
PICKED = list(PICKED_ROWS)
GATHERED = [f for f in range(FEATURES) if f not in PICKED]
NP, NG = len(PICKED), len(GATHERED)
ORDER = GATHERED + PICKED
CHUNK = 125
CHUNKS = [PICKED_ROWS[f] // CHUNK for f in PICKED]
FIRST = [sum(CHUNKS[:k]) for k in range(NP)]
ALL = sum(CHUNKS)

SHIFTS = (FEATURES - 1) // 2
WRAPPED = FEATURES + SHIFTS
PARTS = 3
ANCHORS = FEATURES // PARTS
PAIRS = ANCHORS * SHIFTS
DENSE_IN = [8, 8, 0]
PART_ROWS = [PAIRS + d for d in DENSE_IN]
H1, H2 = 512, 256
H1C, H2C = H1 // 128, H2 // 128

PER_BANK = 4
BANKFULS = [GATHERED[a:a + PER_BANK] for a in range(0, NG, PER_BANK)]
NB = len(BANKFULS)
RING = 7
RAW = 2
RAW_SIZE = max(CHUNKS) * DIM
LAST_PIECES = [(0, 2), (2, 3), (3, 4)]
MLP = H1C + H2C + 1

TRIPS = [(s, 0, TILES_PER_SLAB) for s in range(SLABS - 1)] + [(SLABS - 1, a, b) for a, b in LAST_PIECES]
WHOLE = SLABS - 1

TURN, PICK, DOTS, LAYER = range(4)


def turn(tile, *banks):
    return [(TURN, tile, j) for j in banks]


def pick_of(*features):
    return [(PICK, 0, k) for k in features]


def dots_of(tile, *halves):
    return [(DOTS, tile, h) for h in halves]


def layer_of(*results, piece=None):
    return [(LAYER, piece, m) for m in results]


BANKS = range(NB)
BEFORE = -1
FIRST_STEPS = (turn(1, 0, 1) + dots_of(0, 0, 1) + turn(1, 2, 3, 4) + pick_of(0) + dots_of(1, 0, 1) + pick_of(1)
               + turn(2, *BANKS) + pick_of(2) + dots_of(2, 0) + pick_of(3) + dots_of(2, 1) + pick_of(4)
               + turn(3, *BANKS) + pick_of(5, 6) + dots_of(3, 0) + pick_of(7) + dots_of(3, 1))
STEPS = (turn(0, 0, 1) + pick_of(0) + turn(0, 2, 3, 4) + pick_of(1) + dots_of(0, 0, 1) + layer_of(0)
         + turn(1, 0, 1) + layer_of(1) + turn(1, 2, 3, 4) + pick_of(2) + dots_of(1, 0) + pick_of(3) + dots_of(1, 1)
         + turn(2, 0, 1) + layer_of(2) + turn(2, 2, 3, 4) + pick_of(4) + dots_of(2, 0) + layer_of(3) + pick_of(5)
         + dots_of(2, 1)
         + turn(3, 0, 1) + layer_of(4) + turn(3, 2, 3, 4) + pick_of(6) + dots_of(3, 0) + pick_of(7) + dots_of(3, 1)
         + layer_of(5, 6))
LAST_STEPS = (turn(0, *BANKS) + dots_of(0, 0, 1) + layer_of(0, 1)
              + turn(1, 0, 1) + layer_of(2) + turn(1, 2, 3, 4) + layer_of(3) + dots_of(1, 0) + layer_of(4)
              + dots_of(1, 1) + layer_of(5, 6)
              + turn(2, *BANKS) + dots_of(2, 0, 1) + layer_of(*range(MLP), piece=0)
              + turn(3, *BANKS) + dots_of(3, 0, 1) + layer_of(*range(MLP), piece=1)
              + layer_of(*range(MLP), piece=2))
EARLY = 2


def first_layer_rows():
    rows = []
    dense = FEATURES * (FEATURES - 1) // 2
    for part in range(PARTS):
        for i in range(part * ANCHORS, (part + 1) * ANCHORS):
            for k in range(1, SHIFTS + 1):
                a, b = sorted((ORDER[i], ORDER[(i + k) % FEATURES]))
                rows.append(b * (b - 1) // 2 + a)
        rows += range(dense, dense + DENSE_IN[part])
        dense += DENSE_IN[part]
    return rows


def dense_by_trip(dense):
    tiles = dense.reshape(SLABS, TILES_PER_SLAB, GROUPS, GROUP, DENSE)
    return np.concatenate([tiles[s, a:b].transpose(3, 1, 0, 2).reshape(DENSE, -1) for s, a, b in TRIPS], axis=1)


def constants():
    ident = np.eye(128, dtype=np.float32)
    row_of = np.concatenate([n * np.arange(CHUNK)[:, None] + np.arange(n)[None, :] for n in CHUNKS], axis=1)
    spread = np.repeat(np.eye(NP, dtype=np.float32)[:, :, None], CHUNK, axis=2).reshape(NP, NP * CHUNK)
    return ident, row_of.astype(np.float32), np.ascontiguousarray(spread)


def build(nc, ids, picked_ids, tables, denseT, w1, b1, w2, b2, w3, ident_in, row_of_in, spread_in, out):
    from contextlib import ExitStack

    import concourse.bass as bass
    from concourse import mybir
    from concourse.alu_op_type import AluOpType as ALU

    F32, F16, F32R, I32, U32 = mybir.dt.float32, mybir.dt.float16, mybir.dt.float32r, mybir.dt.int32, mybir.dt.uint32
    ACT = mybir.ActivationFunctionType

    grams = nc.dram_tensor("grams", [FEATURES, WRAPPED, SLAB], F32, kind="Internal").ap()
    last_grams = [nc.dram_tensor(f"last_grams{i}", [FEATURES, WRAPPED, (b - a) * TILE], F32, kind="Internal").ap()
                  for i, (a, b) in enumerate(LAST_PIECES)]
    Q = SLAB // GROUPS

    ctx = ExitStack()
    with ctx:
        def sb(name, shape, dt=F32):
            return ctx.enter_context(nc.sbuf_tensor(name, shape, dt))

        def pb(name):
            return ctx.enter_context(nc.psum_tensor(name, [128, 512], F32))

        def sem(name):
            return ctx.enter_context(nc.semaphore(name))

        ident = sb("ident", [128, 128])
        row_of = sb("row_of", [CHUNK, ALL])
        spread = sb("spread", [NP, NP * CHUNK], F16)
        pids = sb("pids", [NP, SAMPLES], F16)
        index = sb("index", [128, TILES_PER_SLAB, FEATURES], I32)
        rows = sb("rows", [128, 2, NG, DIM])
        hi = sb("hi", [CHUNK, ALL * DIM], F32R)
        lo = sb("lo", [CHUNK, ALL * DIM], F32R)
        onehot = sb("onehot", [CHUNK, RING, SLAB], F32R)
        pickedT = sb("pickedT", [128, 2, NP, SLAB])
        eT = sb("eT", [128, TILE, FEATURES])
        z = sb("z", [128, FEATURES, Q])
        raw = z[:, :, :].rearrange("p j q -> p (j q)")
        zT = sb("zT", [max(PART_ROWS), PARTS, SLAB])
        w1s = sb("w1s", [max(PART_ROWS), PARTS, H1])
        w2s = sb("w2s", [128, H1C, H2])
        w3s = sb("w3s", [128, H2C])
        b1s = sb("b1s", [128, H1C])
        b2s = sb("b2s", [128, H2C])
        h1 = sb("h1", [128, H1C, SLAB])
        h2 = sb("h2", [128, H2C, SLAB])
        ys = sb("ys", [1, SLAB])
        spread_raw = zT[0:NP, :, :].rearrange("p a b -> p (a b)")[:, 0:NP * CHUNK]
        near = h2[0:CHUNK, :, :]
        pids_raw = h1[0:NP, :, :].rearrange("p a b -> p (a b)").bitcast(I32)

        turned = [pb(f"turned{k}") for k in range(2)]
        idb = [pb(f"idb{k}") for k in range(2)]
        pick = pb("pick")
        dots = [pb(f"dots{k}") for k in range(2)]
        layer = pb("layer")
        first_banks = [pick, layer]

        index_loaded = [sem(f"index_loaded{t}") for t in range(TILES_PER_SLAB)]
        gathered = [sem(f"gathered{k}") for k in range(2)]
        ident_loaded = sem("ident_loaded")
        small_loaded = sem("small_loaded")
        weights_loaded = sem("weights_loaded")
        raw_loaded = [sem(f"raw_loaded{k}") for k in range(RAW)]
        hi_split, lo_split = sem("hi_split"), sem("lo_split")
        ids_ready, ids_near, dots_cleared = sem("ids_ready"), sem("ids_near"), sem("dots_cleared")
        turned_filled, turned_copied = sem("turned_filled"), sem("turned_copied")
        idb_filled = sem("idb_filled")
        onehot_ready, onehot_used = sem("onehot_ready"), sem("onehot_used")
        pick_copied, picked_placed = sem("pick_copied"), sem("picked_placed")
        dots_filled, dots_copied = sem("dots_filled"), sem("dots_copied")
        grams_stored, zT_loaded = sem("grams_stored"), sem("zT_loaded")
        layer_filled, layer_copied = sem("layer_filled"), sem("layer_copied")
        y_stored, table_in = sem("y_stored"), sem("table_in")
        waited = sem("waited")

        def raw_of(k):
            return raw[0:CHUNK, (k % RAW) * RAW_SIZE:(k % RAW) * RAW_SIZE + CHUNKS[k] * DIM]

        def table_of(k):
            return slice(FIRST[k] * DIM, (FIRST[k] + CHUNKS[k]) * DIM)

        def layer_place(trip, m):
            if not isinstance(trip, int) or trip < WHOLE:
                return layer, slice(0, SLAB)
            _, t0, t1 = TRIPS[trip]
            return [layer, pick, idb[0], idb[1]][(MLP * (trip - WHOLE) + m) % 4], slice(t0 * TILE, t1 * TILE)

        def used_before(i):
            return i - RING if i >= RING else max(j for j in range(ALL) if j % RING == i) - ALL

        GRAM_STORES, ZT_LOADS = 2 * GROUPS, PARTS + 2

        block = ctx.enter_context(nc.Block())

        @block.gpsimd
        def _(pool):
            def slab(s, first):
                for t in range(TILES_PER_SLAB):
                    n = s * TILES_PER_SLAB + t
                    pool.wait_ge(index_loaded[t], 16 * (s + 1))
                    if not (first and t < 2):
                        pool.wait_ge(turned_filled, NB * (n - 1))
                    pool.sem_inc(waited, 1)
                    for a, f in enumerate(GATHERED):
                        pool.indirect_dma_start(
                            rows[:, t % 2, a, :], None, tables[f],
                            bass.IndirectOffsetOnAxis(ap=index[:, t, f:f + 1].bitcast(U32), axis=0),
                        ).then_inc(gathered[t % 2], 16)

            slab(0, True)
            with pool.Fori(1, SLABS) as s:
                slab(s, False)

        @block.sync
        def _(sp):
            by_tile = ids.rearrange("(n p) f -> p n f", p=TILE)
            tables_by_row = [tables[f].rearrange("(p c) d -> p (c d)", c=c) for f, c in zip(PICKED, CHUNKS)]
            for t in range(TILES_PER_SLAB):
                sp.dma_start(index[:, t, :], by_tile[:, t, :]).then_inc(index_loaded[t], 16)
                if t < RAW:
                    sp.dma_start(raw_of(t), tables_by_row[t]).then_inc(raw_loaded[t], 16)
            for k in range(RAW, NP):
                sp.wait_ge(hi_split, k - RAW + 1)
                sp.wait_ge(lo_split, k - RAW + 1)
                sp.dma_start(raw_of(k), tables_by_row[k]).then_inc(raw_loaded[k % RAW], 16)
            at = 0
            for part, r in enumerate(PART_ROWS):
                sp.dma_start(w1s[0:r, part, :], w1[at:at + r, :]).then_inc(weights_loaded, 16)
                at += r
            sp.dma_start(w2s[:, :, :], w2.rearrange("(c p) n -> p c n", p=128)).then_inc(weights_loaded, 16)
            sp.dma_start(w3s[:, :], w3).then_inc(weights_loaded, 16)
            sp.dma_start(b1s[:, :], b1).then_inc(weights_loaded, 16)
            sp.dma_start(b2s[:, :], b2).then_inc(weights_loaded, 16)

            def next_indices(s):
                for t in range(TILES_PER_SLAB):
                    sp.wait_ge(gathered[t % 2], 16 * NG * (2 * s + t // 2 + 1))
                    sp.sem_inc(waited, 1)
                    sp.dma_start(index[:, t, :], by_tile[:, bass.ds((s + 1) * TILES_PER_SLAB + t, 1), :]
                                 .rearrange("p n f -> p (n f)")).then_inc(index_loaded[t], 16)

            def pairs_to_partitions(trip, first):
                whole = not isinstance(trip, int) or trip < WHOLE
                s, t0, t1 = (trip, 0, TILES_PER_SLAB) if whole else TRIPS[trip]
                sp.wait_ge(dots_copied, 2 * (TILES_PER_SLAB * s + t1))
                sp.sem_inc(waited, 1)
                if not first:
                    sp.wait_ge(zT_loaded, 16 * ZT_LOADS * trip)
                to = grams if whole else last_grams[trip - WHOLE]
                n = (t1 - t0) * TILE
                each = n // GROUPS
                for g in range(GROUPS):
                    for at, width in ((0, FEATURES), (FEATURES, SHIFTS)):
                        sp.dma_start(to[:, at:at + width, g * each:(g + 1) * each],
                                     z[g * 32:g * 32 + FEATURES, 0:width, t0 * GROUP:t1 * GROUP])\
                          .then_inc(grams_stored, 16)
                if not first:
                    sp.wait_ge(layer_filled, MLP * ((trip if whole else WHOLE) - 1) + H1C)
                    sp.sem_inc(waited, 1)
                at = 0
                cols = slice(t0 * TILE, t1 * TILE)
                for part, d in enumerate(DENSE_IN):
                    if d:
                        sp.dma_start(zT[PAIRS:PAIRS + d, part, cols], denseT[at:at + d, bass.ds(s * SLAB + t0 * TILE, n)])\
                          .then_inc(zT_loaded, 16)
                        at += d
                sp.wait_ge(grams_stored, 16 * GRAM_STORES * (trip + 1))
                for part in range(PARTS):
                    i = part * ANCHORS
                    src = bass.AP(to.tensor, (i * WRAPPED + i + 1) * n, [[(WRAPPED + 1) * n, ANCHORS], [n, SHIFTS], [1, n]])
                    sp.dma_start(zT[0:PAIRS, part, cols], src).then_inc(zT_loaded, 16)

            def store_y(trip):
                whole = not isinstance(trip, int) or trip < WHOLE
                s, t0, t1 = (trip, 0, TILES_PER_SLAB) if whole else TRIPS[trip]
                sp.wait_ge(layer_copied, MLP * (trip + 1))
                sp.sem_inc(waited, 1)
                dst = out[bass.ds(s * SLAB + t0 * TILE, (t1 - t0) * TILE), :]
                sp.dma_start(dst.rearrange("(t g q) o -> o g t q", g=GROUPS, q=GROUP),
                             ys[:, t0 * TILE:t1 * TILE].rearrange("o (g t q) -> o g t q", g=GROUPS, q=GROUP))\
                  .then_inc(y_stored, 16)

            next_indices(0)
            pairs_to_partitions(0, True)
            with sp.Fori(1, SLABS - 1) as s:
                next_indices(s)
                pairs_to_partitions(s, False)
                store_y(s - 1)
            pairs_to_partitions(WHOLE, False)
            store_y(WHOLE - 1)
            for trip in range(WHOLE + 1, len(TRIPS)):
                pairs_to_partitions(trip, False)
                store_y(trip - 1)
            store_y(len(TRIPS) - 1)
            sp.wait_ge(y_stored, 16 * len(TRIPS))

        @block.scalar
        def _(act):
            for dst, src in ((row_of[:, :], row_of_in), (spread_raw, spread_in), (pids_raw, picked_ids)):
                act.dma_start(dst, src).then_inc(small_loaded, 16)
            act.dma_start(ident[:, :], ident_in).then_inc(ident_loaded, 16)
            act.wait_ge(dots_cleared, 1)
            nc.scalar.copy(ys[:, 0:1], dots[0][0:1, 0:1]).then_inc(table_in, 1)

            def copy_turned(s, t, j, first):
                n = s * TILES_PER_SLAB + t
                if j == 0 and not (first and t == 0):
                    act.wait_ge(dots_filled, 2 * n)
                act.wait_ge(turned_filled, NB * n + j + 1)
                a, fs = j * PER_BANK, len(BANKFULS[j])
                nc.scalar.copy(eT[:, :, a:a + fs].rearrange("p b f -> p f b"),
                               turned[(NB * t + j) % 2][:, 0:fs * TILE].rearrange("p (f b) -> p f b", f=fs))\
                  .then_inc(turned_copied, 1)

            def place_picked(s, t):
                act.wait_ge(pick_copied, NP * (s + 1))
                nc.scalar.copy(eT[:, :, NG:FEATURES].rearrange("p b f -> p f b"),
                               pickedT[:, bass.ds(s % 2, 1), :, t * TILE:(t + 1) * TILE]
                               .rearrange("p o f b -> p (o f) b")).then_inc(picked_placed, 1)

            def copy_pick(s, k, bank):
                act.wait_ge(onehot_used, ALL * s + FIRST[k] + CHUNKS[k])
                nc.scalar.copy(pickedT[:, bass.ds(s % 2, 1), k, :].rearrange("p o b -> p (o b)"), bank[:, :])\
                  .then_inc(pick_copied, 1)

            def copy_layer(trip, m):
                act.wait_ge(layer_filled, MLP * trip + m + 1)
                bank, cols = layer_place(trip, m)
                src = bank[:, 0:cols.stop - cols.start]
                if m < H1C:
                    op = nc.scalar.activation(h1[:, m, cols], src, ACT.Relu, bias=b1s[:, m:m + 1])
                elif m < H1C + H2C:
                    op = nc.scalar.activation(h2[:, m - H1C, cols], src, ACT.Relu, bias=b2s[:, m - H1C:m - H1C + 1])
                else:
                    if not isinstance(trip, int) or trip > 0:
                        act.wait_ge(y_stored, 16 * (trip if not isinstance(trip, int) or trip < WHOLE else WHOLE))
                    op = nc.scalar.copy(ys[:, cols], src[0:1, :])
                op.then_inc(layer_copied, 1)

            def copy_dots(s, t, h, first):
                if t == 0 and h == 0 and not first:
                    act.wait_ge(grams_stored, 16 * GRAM_STORES * s)
                act.wait_ge(dots_filled, 2 * (s * TILES_PER_SLAB + t) + h + 1)
                q = t % TILES_PER_SLAB * GROUP + h * HALF
                nc.scalar.copy(z[:, :, q:q + HALF].rearrange("p j q -> p q j"),
                               dots[h][:, 0:HALF * FEATURES].rearrange("p (q j) -> p q j", q=HALF))\
                  .then_inc(dots_copied, 1)

            def slab(s, steps, first):
                for kind, at, x in steps:
                    if kind == TURN:
                        copy_turned(s, at, x, first)
                        if x == 0:
                            place_picked(s, at)
                    elif kind == PICK:
                        copy_pick(s + 1, x, pick)
                    elif kind == DOTS:
                        copy_dots(s, at, x, first)
                    elif at is None:
                        copy_layer(s - 1, x)
                    else:
                        copy_layer(WHOLE + at, x)

            def copy_ids(k):
                act.wait_ge(idb_filled, k + 1)
                if k >= 2:
                    act.wait_ge(onehot_ready, FIRST[k - 1])
                nc.scalar.copy(near[:, k % 2, :], idb[k % 2][0:CHUNK, :]).then_inc(ids_near, 1)

            def split_high(k):
                act.wait_ge(raw_loaded[k % RAW], 16 * (k // RAW + 1))
                nc.scalar.copy(hi[:, table_of(k)], raw_of(k)).then_inc(hi_split, 1)

            split_high(0)
            copy_ids(0)
            split_high(1)
            copy_ids(1)
            for k in range(NP):
                copy_pick(0, k, first_banks[k % 2])
                if k == EARLY:
                    for j in BANKS:
                        copy_turned(0, 0, j, True)
                if k + 2 < NP:
                    copy_ids(k + 2)
                    split_high(k + 2)
            place_picked(0, 0)
            act.wait_ge(weights_loaded, 16 * (PARTS + 4))
            slab(0, FIRST_STEPS, True)
            with act.Fori(1, SLABS - 1) as s:
                slab(s, STEPS, False)
            slab(SLABS - 1, LAST_STEPS, False)

        @block.vector
        def _(dve):
            for d in dots:
                nc.vector.memset(d[:, :], 0.0).then_inc(dots_cleared, 1)
            dve.wait_ge(small_loaded, 48)
            nc.vector.tensor_copy(spread[:, :], spread_raw).then_inc(ids_ready, 1)
            nc.vector.tensor_copy(pids[:, :], pids_raw).then_inc(ids_ready, 1)

            def one_hots(s, k, first):
                if first:
                    dve.wait_ge(ids_near, k + 1)
                    spread_out = near[:, k % 2, :]
                else:
                    dve.wait_ge(idb_filled, NP * s + k + 1)
                    spread_out = idb[k % 2][0:CHUNK, :]
                for i in range(FIRST[k], FIRST[k] + CHUNKS[k]):
                    if not (first and i < RING):
                        dve.wait_ge(onehot_used, ALL * s + used_before(i) + 1)
                    nc.vector.tensor_scalar(onehot[:, i % RING, :], spread_out, row_of[:, i:i + 1], None,
                                            ALU.is_equal).then_inc(onehot_ready, 1)

            for k in range(NP):
                dve.wait_ge(hi_split, k + 1)
                nc.vector.tensor_tensor(lo[:, table_of(k)], raw_of(k), hi[:, table_of(k)].bitcast(F32),
                                        ALU.subtract).then_inc(lo_split, 1)
                one_hots(0, k, True)
            with dve.Fori(1, SLABS) as s:
                for k in range(NP):
                    one_hots(s, k, False)

        @block.tensor
        def _(pe):
            def turn_rows(s, t, j, first):
                n = s * TILES_PER_SLAB + t
                if j == 0:
                    pe.wait_ge(gathered[t % 2], 16 * NG * (2 * s + t // 2 + 1))
                if not (first and t == 0 and j < 2):
                    pe.wait_ge(turned_copied, NB * n + j - 1)
                for c in range(len(BANKFULS[j])):
                    op = nc.tensor.transpose(turned[(NB * t + j) % 2][:, c * TILE:(c + 1) * TILE],
                                             rows[:, t % 2, j * PER_BANK + c, :], ident[:, :])
                op.then_inc(turned_filled, 1)

            def spread_ids(s, k, first):
                if not (first and k < 2):
                    pe.wait_ge(onehot_ready, ALL * s + (FIRST[k - 1] if k >= 2 else 0))
                    pe.sem_inc(waited, 1)
                nc.tensor.matmul(idb[k % 2][0:CHUNK, :], spread[:, k * CHUNK:(k + 1) * CHUNK],
                                 pids[:, bass.ds(s * SLAB, SLAB)], start=True, stop=True).then_inc(idb_filled, 1)

            def pick_feature(s, k, bank, first):
                if k + 1 < NP:
                    spread_ids(s, k + 1, first)
                if not first or k >= 2:
                    pe.wait_ge(pick_copied, k - 1 if first else NP * s + k)
                if first:
                    pe.wait_ge(lo_split, k + 1)
                for c in range(CHUNKS[k]):
                    i = FIRST[k] + c
                    pe.wait_ge(onehot_ready, ALL * s + i + 1)
                    part = slice(i * DIM, (i + 1) * DIM)
                    nc.tensor.matmul(bank[:, :], hi[:, part], onehot[:, i % RING, :], start=c == 0, stop=False)
                    nc.tensor.matmul(bank[:, :], lo[:, part], onehot[:, i % RING, :], start=False,
                                     stop=c == CHUNKS[k] - 1).then_inc(onehot_used, 1)

            def dot_products(s, t, h, first):
                n = s * TILES_PER_SLAB + t
                if h == 0:
                    pe.wait_ge(turned_copied, NB * (n + 1))
                    pe.wait_ge(picked_placed, n + 1)
                if first and t == 0:
                    pe.wait_ge(dots_cleared, h + 1)
                else:
                    pe.wait_ge(dots_copied, 2 * n + h - 1)
                for q in range(HALF):
                    for g in range(GROUPS):
                        b = g * GROUP + h * HALF + q
                        op = nc.tensor.matmul(dots[h][g * 32:g * 32 + FEATURES, q * FEATURES:(q + 1) * FEATURES],
                                              eT[:, b, :], eT[:, b, :], start=True, stop=True, tile_position=(0, 32 * g))
                op.then_inc(dots_filled, 1)

            def dense_layer(trip, m):
                if m == 0:
                    pe.wait_ge(zT_loaded, 16 * ZT_LOADS * (trip + 1))
                bank, cols = layer_place(trip, m)
                if not isinstance(trip, int) or trip < WHOLE:
                    if not (isinstance(trip, int) and trip == 0 and m == 0):
                        pe.wait_ge(layer_copied, MLP * trip + m)
                else:
                    bank_free = max(MLP * trip + m - 3, MLP * WHOLE)
                    layer_read = MLP * trip + (0 if m < H1C else H1C if m < H1C + H2C else H1C + H2C)
                    pe.wait_ge(layer_copied, max(bank_free, layer_read))
                if m < H1C:
                    terms = [(w1s[0:r, p, m * 128:(m + 1) * 128], zT[0:r, p, cols]) for p, r in enumerate(PART_ROWS)]
                elif m < H1C + H2C:
                    a = (m - H1C) * 128
                    terms = [(w2s[:, c, a:a + 128], h1[:, c, cols]) for c in range(H1C)]
                else:
                    terms = [(w3s[:, c:c + 1], h2[:, c, cols]) for c in range(H2C)]
                to = bank[0:128 if m < MLP - 1 else 1, 0:cols.stop - cols.start]
                for i, (w, x) in enumerate(terms):
                    op = nc.tensor.matmul(to, w, x, start=i == 0, stop=i == len(terms) - 1)
                op.then_inc(layer_filled, 1)

            def slab(s, steps, first):
                if any(kind == PICK for kind, _, _ in steps):
                    spread_ids(s + 1, 0, False)
                for kind, at, x in steps:
                    if kind == TURN:
                        turn_rows(s, at, x, first)
                    elif kind == PICK:
                        pick_feature(s + 1, x, pick, False)
                    elif kind == DOTS:
                        dot_products(s, at, x, first)
                    elif at is None:
                        dense_layer(s - 1, x)
                    else:
                        dense_layer(WHOLE + at, x)

            pe.wait_ge(ids_ready, 2)
            spread_ids(0, 0, True)
            for k in range(NP):
                pick_feature(0, k, first_banks[k % 2], True)
                if k == EARLY:
                    pe.wait_ge(ident_loaded, 16)
                    for j in BANKS:
                        turn_rows(0, 0, j, True)
            pe.wait_ge(weights_loaded, 16 * (PARTS + 4))
            slab(0, FIRST_STEPS, True)
            with pe.Fori(1, SLABS - 1) as s:
                slab(s, STEPS, False)
            pe.wait_ge(pick_copied, NP * SLABS)
            slab(SLABS - 1, LAST_STEPS, False)


def kernel(**inputs):
    import concourse.bacc as bacc
    from concourse import mybir
    from concourse.bass_utils import run_bass_kernel_spmd

    nc = bacc.Bacc("TRN2", target_bir_lowering=False, num_devices=1)
    ids = np.ascontiguousarray(inputs["ids"])
    w1 = np.asarray(inputs["W_top1"])
    ident, row_of, spread = constants()
    arrays = {
        "ids": ids,
        "picked_ids": np.ascontiguousarray(ids.T[PICKED]),
        "denseT": dense_by_trip(np.asarray(inputs["dense_ctx"])),
        "w1": np.ascontiguousarray(w1[first_layer_rows()]),
        "b1": np.ascontiguousarray(np.asarray(inputs["b_top1"]).reshape(H1C, 128).T),
        "w2": np.ascontiguousarray(inputs["W_top2"]),
        "b2": np.ascontiguousarray(np.asarray(inputs["b_top2"]).reshape(H2C, 128).T),
        "w3": np.ascontiguousarray(np.asarray(inputs["W_top3"]).reshape(H2C, 128).T),
        "ident_in": ident, "row_of_in": row_of, "spread_in": spread,
    }
    arrays |= {f"tbl_{f}": np.ascontiguousarray(inputs[f"tbl_{f}"]) for f in range(FEATURES)}
    aps = {n: nc.dram_tensor(f"in_{n}", a.shape, mybir.dt.from_np(a.dtype), kind="ExternalInput").ap()
           for n, a in arrays.items()}
    tables = [aps.pop(f"tbl_{f}") for f in range(FEATURES)]
    out = nc.dram_tensor("out_y", [SAMPLES, 1], mybir.dt.float32, kind="ExternalOutput").ap()
    build(nc, tables=tables, out=out, **aps)
    result = run_bass_kernel_spmd(nc, [{f"in_{n}": a for n, a in arrays.items()}], core_ids=[0])
    return result.results[0]["out_y"]
```
